# Optimizing a Trainium2 kernel written in Bass

```python
import numpy as np
import jax
import jax.numpy as jnp

def _softmax(x, axis=-1):
    return jax.nn.softmax(x, axis=axis)

def _gelu(x):
    return jax.nn.gelu(x, approximate=True)

def _silu(x):
    return jax.nn.silu(x)

def _sigmoid(x):
    return jax.nn.sigmoid(x)

def _layernorm(x, axis=-1, eps=1e-05):
    m = jnp.mean(x, axis=axis, keepdims=True)
    v = jnp.var(x, axis=axis, keepdims=True)
    return (x - m) / jnp.sqrt(v + eps)

def _scatter_add(tgt, idx, src, axis=0):
    return tgt.at[idx].add(src)

def _segment_sum(src, seg, n):
    return jax.ops.segment_sum(src, seg, n)
kernel_name = 'mk_xattn_ffn_d1_seqx_r4_2ed512'

def setup_inputs(seed: int=0):
    np.random.seed(seed)
    _w = jnp.asarray

    def _rec_inputs():
        import jax
        import jax.numpy as jnp
        _rk = jax.random.key(seed)
        x = 7.22e-05 + 1 * jax.random.normal(jax.random.fold_in(_rk, 1), (128, 128, 256), jnp.float32)
        _lenS = 128 - jax.random.randint(jax.random.fold_in(_rk, 7), (128,), 0, max(1, 128 // 4) + 1, jnp.int32)
        _lenS2 = 128 - jax.random.randint(jax.random.fold_in(_rk, 8), (128,), 0, max(1, 128 // 4) + 1, jnp.int32)
        _ctx_1024P = jax.random.normal(jax.random.fold_in(_rk, 11), (128, 16, 256), jnp.float32)
        _ctx_1024c = jax.random.dirichlet(jax.random.fold_in(_rk, 511), 0.3 * jnp.ones((16,), jnp.float32), (128, 128))
        _ctx_1024t = jnp.einsum('bsk,bkd->bsd', _ctx_1024c, _ctx_1024P)
        _ctx_1024t = _ctx_1024t * jax.lax.rsqrt(jnp.mean(jnp.square(_ctx_1024t)) + 1e-12) * 0.953939
        ctx_1024 = 4.13588e-05 + 0.999923 * (_ctx_1024t + 0.3 * jax.random.normal(jax.random.fold_in(_rk, 611), (128, 128, 256), jnp.float32))
        return (x, ctx_1024)
    x, ctx_1024 = _rec_inputs()

    def _L0_xattn_setup():
        import jax, jax.numpy as jnp
        import numpy as np
        EMB_DIM = 256
        NUM_HEADS = 16
        HEAD_DIM = EMB_DIM // NUM_HEADS
        key = jax.random.key(seed)
        ks = jax.random.split(key, 7)
        B, S, E = (4, 512, EMB_DIM)
        scale = 1.0 / np.sqrt(E)
        return {'q': jax.random.normal(ks[0], (B, S, E), dtype=jnp.float32), 'k': jax.random.normal(ks[1], (B, S, E), dtype=jnp.float32), 'v': jax.random.normal(ks[2], (B, S, E), dtype=jnp.float32), 'Wq': jax.random.normal(ks[3], (E, E), dtype=jnp.float32) * scale, 'Wk': jax.random.normal(ks[4], (E, E), dtype=jnp.float32) * scale, 'Wv': jax.random.normal(ks[5], (E, E), dtype=jnp.float32) * scale, 'Wo': jax.random.normal(ks[6], (E, E), dtype=jnp.float32) * scale}
    _L0_xattn_all = _L0_xattn_setup()
    _L0_xattn_in = {k: v for k, v in _L0_xattn_all.items() if k in ('Wq', 'Wk', 'Wv', 'Wo')}
    del _L0_xattn_all

    def _L0_ffn_setup():
        import jax, jax.numpy as jnp
        import numpy as np
        H_DIM, E_DIM = (256, 128)
        N_SHARED, N_ROUTED, TOP_K = (2, 16, 4)
        B, S = (4, 512)
        key = jax.random.key(seed)
        ks = jax.random.split(key, 6)
        sc = 1.0 / np.sqrt(H_DIM)
        ec = 1.0 / np.sqrt(E_DIM)
        return {'x': jax.random.normal(ks[0], (B, S, H_DIM), dtype=jnp.float32), 'shared_up': jax.random.uniform(ks[1], (N_SHARED, E_DIM, H_DIM), jnp.float32, -sc, sc), 'shared_down': jax.random.uniform(ks[2], (N_SHARED, H_DIM, E_DIM), jnp.float32, -ec, ec), 'routed_up': jax.random.uniform(ks[3], (N_ROUTED, E_DIM, H_DIM), jnp.float32, -sc, sc), 'routed_down': jax.random.uniform(ks[4], (N_ROUTED, H_DIM, E_DIM), jnp.float32, -ec, ec), 'router_w': jax.random.uniform(ks[5], (N_ROUTED, H_DIM), jnp.float32, -sc, sc)}
    _L0_ffn_all = _L0_ffn_setup()
    _L0_ffn_in = {k: v for k, v in _L0_ffn_all.items() if k in ('shared_up', 'shared_down', 'routed_up', 'routed_down', 'router_w')}
    del _L0_ffn_all
    return {'x': x, 'ctx_1024': ctx_1024, 'L0_xattn_Wq': _L0_xattn_in['Wq'], 'L0_xattn_Wk': _L0_xattn_in['Wk'], 'L0_xattn_Wv': _L0_xattn_in['Wv'], 'L0_xattn_Wo': _L0_xattn_in['Wo'], 'L0_ffn_shared_up': _L0_ffn_in['shared_up'], 'L0_ffn_shared_down': _L0_ffn_in['shared_down'], 'L0_ffn_routed_up': _L0_ffn_in['routed_up'], 'L0_ffn_routed_down': _L0_ffn_in['routed_down'], 'L0_ffn_router_w': _L0_ffn_in['router_w']}

def reference(x, ctx_1024, L0_xattn_Wq, L0_xattn_Wk, L0_xattn_Wv, L0_xattn_Wo, L0_ffn_shared_up, L0_ffn_shared_down, L0_ffn_routed_up, L0_ffn_routed_down, L0_ffn_router_w):
    import jax
    import jax.numpy as jnp

    def _L0_xattn_ref(q, k, v, Wq, Wk, Wv, Wo):
        import jax, jax.numpy as jnp
        import numpy as np
        EMB_DIM = 256
        NUM_HEADS = 16
        HEAD_DIM = EMB_DIM // NUM_HEADS
        B, S, E = q.shape
        H, D = (NUM_HEADS, HEAD_DIM)
        qh = (q @ Wq.T).reshape(B, S, H, D).transpose(0, 2, 1, 3)
        kh = (k @ Wk.T).reshape(B, S, H, D).transpose(0, 2, 1, 3)
        vh = (v @ Wv.T).reshape(B, S, H, D).transpose(0, 2, 1, 3)
        scores = jnp.einsum('bhse,bhte->bhst', qh, kh) / jnp.sqrt(jnp.float32(D))
        attn = jax.nn.softmax(scores, axis=-1)
        out = jnp.einsum('bhst,bhtd->bshd', attn, vh).reshape(B, S, E)
        return out @ Wo.T

    def _L0_ffn_ref(x, shared_up, shared_down, routed_up, routed_down, router_w):
        import jax, jax.numpy as jnp
        import numpy as np
        H_DIM, E_DIM = (256, 128)
        N_SHARED, N_ROUTED, TOP_K = (2, 16, 4)
        B, S = (4, 512)
        b, s, h = x.shape
        xt = x.reshape(-1, h)
        up_s = jnp.einsum('th,seh->tse', xt, shared_up)
        shared = jnp.einsum('tse,she->th', jax.nn.gelu(up_s, approximate=False), shared_down)
        probs = jax.nn.softmax(xt @ router_w.T, axis=-1)
        topk_p, topk_i = jax.lax.top_k(probs, TOP_K)
        gate = jnp.zeros_like(probs).at[jnp.arange(xt.shape[0])[:, None], topk_i].add(topk_p)
        up_r = jnp.einsum('th,reh->tre', xt, routed_up)
        act = jax.nn.gelu(up_r, approximate=False) * gate[:, :, None]
        routed = jnp.einsum('tre,rhe->th', act, routed_down)
        return (shared + routed).reshape(b, s, h)
    x = x + _L0_xattn_ref(_layernorm(x, axis=-1), ctx_1024, ctx_1024, L0_xattn_Wq, L0_xattn_Wk, L0_xattn_Wv, L0_xattn_Wo)
    x = x + _L0_ffn_ref(_layernorm(x, axis=-1), L0_ffn_shared_up, L0_ffn_shared_down, L0_ffn_routed_up, L0_ffn_routed_down, L0_ffn_router_w)
    return x

_drawn_inputs = setup_inputs


def setup_inputs(seed=0):
    import zlib

    import numpy as np

    out = dict(_drawn_inputs(seed))
    spreads = {}
    factors = {}
    for name, (base, spread) in spreads.items():
        noise = np.random.default_rng([zlib.crc32(name.encode()), seed]).standard_normal(out[name].shape)
        drawn = base * np.exp(spread * noise) if base else spread * noise
        out[name] = jnp.asarray(drawn.astype(out[name].dtype))
    for name, factor in factors.items():
        out[name] = (out[name] * factor).astype(out[name].dtype)
    return out
```

```python
import concourse.bass as bass
from concourse import mybir
from contextlib import ExitStack

F32 = mybir.dt.float32
F32R = mybir.dt.float32r
BF16 = mybir.dt.bfloat16
F16 = mybir.dt.float16
ALU = mybir.AluOpType
ACT = mybir.ActivationFunctionType
AX = mybir.AxisListType

P = 128
B, S, E = 128, 128, 256
KC = E // P
NH, HD = 16, 16
GT = 4
G = B // GT
T = GT * P
NSH, NRT, TOPK, EH = 2, 16, 4, 128
NX = NSH + NRT
VP = HD + 1
VW = 3 * VP
SCALE = 1.0 / HD ** 0.5
EPS = 1e-5

FRONT = [("K", 0), ("K", 1), ("V", 0), ("V", 1), ("XT", 0), ("Q", 0), ("Q", 1)]


def tile_stages(i):
    late = [("XT2", i - 1)] if i else []
    later = [("RT", i - 1)] if i else []
    return [[("S", i)], [("T", i)], [("PV", i)] + late, [("OT", i)] + later, [("OP", i)]]


EXPERTS = []
for _r in range(NX):
    EXPERTS.append(("UP", _r))
    if _r >= 2:
        EXPERTS.append(("DN", _r - 2))
EXPERTS += [("DN", NX - 2), ("DN", NX - 1), ("FIN", 0)]


def interleave():
    ex = list(EXPERTS)
    out = []

    def give(n):
        for _ in range(n):
            out.append(ex.pop(0))

    out.extend([("CTX", 0), ("K", 0)])
    give(1)
    out.extend([("K", 1), ("V", 0), ("V", 1), ("LN1", 0)])
    give(3)
    out.extend([("XT", 0)])
    give(1)
    out.extend([("Q", 0), ("Q", 1)])
    give(1)
    for i in range(GT):
        s, t, pv, ot, op = tile_stages(i)
        for part, n in ((s, 2), (t, 2), (pv, 1), (ot, 1), (op, 1)):
            out.extend(part)
            give(n if len(ex) > 5 else 0)
    out.extend([("XT2", GT - 1)])
    give(1)
    out.extend([("RT", GT - 1), ("ROUTE", 0)])
    give(len(ex))
    out.extend([("GT", 0)])
    return out


STEP = interleave()
ATTN_STAGES = ("CTX", "K", "V", "LN1", "XT", "Q", "S", "T", "PV", "OT", "OP", "XT2", "RT", "ROUTE", "GT")
ATTN_ONLY = [s for s in STEP if s[0] in ATTN_STAGES]
EXPERTS_ONLY = [s for s in STEP if s[0] not in ATTN_STAGES]

BANKS_OF = {"K": lambda n: [n], "V": lambda n: [2 + n], "XT": lambda n: [0, 1], "Q": lambda n: [2 + n],
            "S": lambda n: [0, 1, 2, 3], "T": lambda n: [0, 1, 2, 3], "PV": lambda n: [0, 1],
            "OT": lambda n: [2], "OP": lambda n: [3], "XT2": lambda n: [2], "RT": lambda n: [3],
            "GT": lambda n: [2]}
BANK_USES = [[s for s in ATTN_ONLY if s[0] in BANKS_OF and b in BANKS_OF[s[0]](s[1])] for b in range(4)]


def nth_use(b, stage, n):
    return BANK_USES[b].index((stage, n)) + 1


def program(nc, x, ctx_t, wq, wk, wv, wo, sup, sdn, rup, rdn, rw, out):
    es = ExitStack()
    with es:
        def sb(name, shape, dt=F32):
            return es.enter_context(nc.sbuf_tensor(name, shape, dt))

        def sem(name):
            return es.enter_context(nc.semaphore(name))

        ident = sb("ident", [P, P])
        neg_half = sb("neg_half", [P, GT])
        mask = sb("mask", [P, 2])
        sel = sb("sel", [P, NRT], F32R)
        self32 = sb("self32", [P, NRT])
        wp = [sb(f"wp{k}", [P, 4, KC, E], F32R) for k in "hl"]
        wu = [sb(f"wu{k}", [P, KC, NX, EH], F32R) for k in "hl"]
        wd = [sb(f"wd{k}", [P, NX, E], F32R) for k in "hl"]
        wr = sb("wr", [P, KC, NRT])
        xy = [sb(f"xy{p}", [P, GT, E]) for p in range(2)]
        cg = sb("cg", [P, KC, T])
        at = [sb(f"at{k}", [P, KC, T], F32R) for k in "hl"]
        xn = sb("xn", [P, 2, E])
        qt = sb("qt", [P, KC, T])
        km = sb("km", [P, KC, GT, 2, P])
        vrest = sb("vrest", [P, 2, 2 * E])
        vp = sb("vp", [P, GT, NH, VW], BF16)
        pr = sb("pr", [P, NH, P])
        ph = sb("ph", [P, NH, P], F16)
        pl = sb("pl", [P, NH, P], F16)
        od = sb("od", [P, NH, VP])
        o = sb("o", [P, NH, HD])
        ot = [sb(f"ot{k}", [P, KC, P], F32R) for k in "hl"]
        xn2 = sb("xn2", [P, E])
        t32 = sb("t32", [P, KC, P])
        x2 = [[sb(f"x2{k}{p}", [P, KC, T], F32R) for k in "hl"] for p in range(2)]
        gt = [sb(f"gt{p}", [P, T], F32R) for p in range(2)]
        act = sb("act", [P, 3, T])
        hh = sb("hh", [P, 3, T], F32R)
        hl = sb("hl", [P, 3, T], F32R)
        ft = sb("ft", [P, KC, T])
        ob = sb("ob", [P, GT, E])
        st1, mv1, ve1, rs1 = sb("st1", [P, GT, 6]), sb("mv1", [P, GT, 2]), sb("ve1", [P, GT]), sb("rs1", [P, GT])
        st2, mv2, ve2, rs2 = sb("st2", [P, 6]), sb("mv2", [P, 2]), sb("ve2", [P, 1]), sb("rs2", [P, 1])
        mx, nm, rd = sb("mx", [P, NH]), sb("nm", [P, NH]), sb("rd", [P, NH])
        lg, lm, nlm = sb("lg", [P, GT, NRT]), sb("lm", [P, GT, 8]), sb("nlm", [P, GT])
        ex, rsum, rrec = sb("ex", [P, GT, NRT]), sb("rsum", [P, GT]), sb("rrec", [P, GT])
        prob = sb("prob", [P, GT, NRT + TOPK])
        top = sb("top", [P, GT, 8])
        rest = sb("rest", [P, GT, NRT + TOPK])
        gate = sb("gate", [P, GT, NRT])
        pad = sb("pad", [P, 1])
        gs = sb("gs", [P, GT, 2 * NRT], F32R)

        A = [es.enter_context(nc.psum_tensor(f"A{b}", [P, 512], F32)) for b in range(4)]
        U = es.enter_context(nc.psum_tensor("U", [P, 512], F32))
        W = es.enter_context(nc.psum_tensor("W", [P, 512], F32))
        FB = [es.enter_context(nc.psum_tensor(f"F{c}", [P, 512], F32)) for c in range(KC)]

        w_in = [sem(f"w_in{k}") for k in range(2)]
        router_in = sem("router_in")
        w_hi = sem("w_hi")
        w_split = sem("w_split")
        const0 = sem("const0")
        const = sem("const")
        sel_set = sem("sel_set")
        dve_const = sem("dve_const")
        pool_set = sem("pool_set")
        x_in = [sem(f"x_in{p}") for p in range(2)]
        ctx_in = sem("ctx_in")
        stored = sem("stored")
        fillA = [sem(f"fillA{b}") for b in range(4)]
        drainA = [sem(f"drainA{b}") for b in range(4)]
        KA = [len(u) for u in BANK_USES]
        ctx_hi, ctx_lo = sem("ctx_hi"), sem("ctx_lo")
        v_hi, v_rest, v_mid, v_parts = sem("v_hi"), sem("v_rest"), sem("v_mid"), sem("v_parts")
        ln1_st, ln1_mv, ln1_ve, ln1_rs = sem("ln1_st"), sem("ln1_mv"), sem("ln1_ve"), sem("ln1_rs")
        xn_ready, xn_used = sem("xn_ready"), sem("xn_used")
        xt_hi = sem("xt_hi")
        k_even = sem("k_even")
        mx_ready, nm_ready, p_hi = sem("mx_ready"), sem("nm_ready"), sem("p_hi")
        od_ready, rd_ready, o_ready, ot_hi = sem("od_ready"), sem("rd_ready"), sem("o_ready"), sem("ot_hi")
        ln2_st, ln2_mv, ln2_ve, ln2_rs = sem("ln2_st"), sem("ln2_mv"), sem("ln2_ve"), sem("ln2_rs")
        xn2_ready, x2_hi, x2_lo = sem("xn2_ready"), sem("x2_hi"), sem("x2_lo")
        rt_step, rt_exp = sem("rt_step"), sem("rt_exp")
        gate_set = sem("gate_set")
        gates = sem("gates")
        KR = 8
        upF, gelu, bcast, gated = sem("up_filled"), sem("gelu_done"), sem("bcast_filled"), sem("w_drained")
        h_hi, h_lo, dn_done = sem("h_hi"), sem("h_lo"), sem("dn_done")
        f_evict, fin_fill, fin_add = sem("f_evict"), sem("fin_fill"), sem("fin_add")

        block = es.enter_context(nc.Block())
        NP = 6
        stage = [pr[:, :, :].rearrange("p a b -> p (a b)"), km[:, :, :, :, :].rearrange("p c t e n -> p (c t e n)")]

        def weight_pieces():
            c = "(c p)"
            pieces = [[((k, k * KC * E), w.rearrange(f"{c} n -> p c n", p=P), lambda t, k=k: t[:, k, :, :], (KC, E))
                       for k, w in enumerate((wq, wk, wv, wo))]]
            pieces.append([((0, 0), sup.rearrange(f"{c} s e -> p c (s e)", p=P),
                            lambda t: t[:, :, 0:NSH, :].rearrange("p c s e -> p c (s e)"), (KC, NSH * EH)),
                           ((1, KC * NSH * EH), sdn, lambda t: t[:, 0:NSH, :], (NSH, E))])
            half = NRT // 2
            for k in range(2):
                pieces.append([((0, 0), rup.rearrange(f"{c} r e -> p c r e", p=P)[:, :, k * half:(k + 1) * half, :]
                                .rearrange("p c r e -> p c (r e)"),
                                lambda t, k=k: t[:, :, NSH + k * half:NSH + (k + 1) * half, :]
                                .rearrange("p c r e -> p c (r e)"), (KC, half * EH))])
            for k in range(2):
                pieces.append([((1, 0), rdn[:, k * half:(k + 1) * half, :],
                                lambda t, k=k: t[:, NSH + k * half:NSH + (k + 1) * half, :], (half, E))])
            return pieces

        PIECES = weight_pieces()
        TARGET = [lambda m: wp, lambda m: wd if m else wu, lambda m: wu, lambda m: wu, lambda m: wd, lambda m: wd]

        def staged(n, off, shape):
            a, b = shape
            return stage[n % 2][:, off:off + a * b].rearrange("p (a b) -> p a b", a=a)

        def wait(eng, s, v):
            if isinstance(v, int) and v <= 0:
                return
            eng.wait_ge(s, v)

        def wait_apart(s, v):
            nc.vector.wait_ge(s, v)
            nc.vector.memset(pad[:, :], 0.0)

        def wait_filled(eng, g, b, stg, n):
            eng.wait_ge(fillA[b], g * KA[b] + nth_use(b, stg, n))

        def wait_drained(eng, g, b, stg, n):
            eng.wait_ge(drainA[b], g * KA[b] + nth_use(b, stg, n))

        def wait_free(eng, g, b, stg, n):
            wait(eng, drainA[b], g * KA[b] + nth_use(b, stg, n) - 1)

        def run_steps(eng, both):
            both(ATTN_ONLY, 0)
            both(STEP, 1)
            with eng.Fori(0, (G - 2) // 2) as i:
                both(STEP, i * 2 + 2, 0)
                both(STEP, i * 2 + 3, 1)
            both(EXPERTS_ONLY, G)

        @block.sync
        def _(sp):
            for n in range(NP):
                if n >= 2:
                    sp.wait_ge(w_split, n - 1)
                for (_, off), src, _, shape in PIECES[n]:
                    sp.dma_start(staged(n, off, shape), src).then_inc(w_in[n % 2], 16)
            sp.dma_start(wr[:, :, :], rw.rearrange("(c p) r -> p c r", p=P)).then_inc(router_in, 16)

            def load_x(g, p):
                sp.dma_start(xy[p][:, :, :], x[bass.ds(g * GT, GT), :, :].rearrange("b s e -> s b e")).then_inc(x_in[p], 16)

            def load_ctx(g):
                sp.dma_start(cg[:, :, :], ctx_t[:, bass.ds(g * T, T)].rearrange("(c p) t -> p c t", p=P)).then_inc(ctx_in, 16)

            def store(f):
                for k in range(2):
                    sp.wait_ge(fin_add, f * 2 + k + 1)
                    sp.dma_start(out[bass.ds(f * GT + 2 * k, 2), :, :].rearrange("b s e -> s b e"),
                                 ob[:, 2 * k:2 * k + 2, :]).then_inc(stored, 16)

            def step(g, p, last=False):
                if not last:
                    sp.wait_ge(ctx_lo, g + 1)
                    load_ctx(g + 1)
                store(g - 1)
                if not last:
                    load_x(g + 1, 1 - p)

            load_ctx(0)
            load_x(0, 0)
            sp.wait_ge(ctx_lo, 1)
            load_ctx(1)
            load_x(1, 1)
            step(1, 1)
            with sp.Fori(0, (G - 4) // 2) as i:
                step(i * 2 + 2, 0)
                step(i * 2 + 3, 1)
            step(G - 2, 0)
            step(G - 1, 1, last=True)
            store(G - 1)
            sp.wait_ge(stored, 32 * G)

        @block.tensor
        def _(pe):
            mm, tr = nc.tensor.matmul, nc.tensor.transpose

            def three(dst, wh, wl, mh, ml, first=True, last=True):
                passes = [(w(c), m(c)) for c in range(KC) for w, m in ((wh, mh), (wh, ml), (wl, mh))]
                for k, (w, m) in enumerate(passes):
                    ins = mm(dst, w, m, start=first and k == 0, stop=last and k == len(passes) - 1)
                return ins

            def proj(which, c_out):
                return [lambda c, k=k: wp[k][:, which, c, c_out * P:(c_out + 1) * P] for k in range(2)]

            def K(g, c):
                if c == 0:
                    pe.wait_ge(ctx_hi, g + 1)
                    pe.wait_ge(ctx_lo, g + 1)
                wait_free(pe, g, c, "K", c)
                three(A[c][:, :], *proj(1, c), lambda k: at[0][:, k, :], lambda k: at[1][:, k, :]).then_inc(fillA[c], 1)

            def V(g, n):
                wait_free(pe, g, 2 + n, "V", n)
                for k in range(2):
                    tok = slice((2 * n + k) * P, (2 * n + k + 1) * P)
                    ins = three(A[2 + n][:, k * E:(k + 1) * E],
                                lambda c: at[0][:, c, tok], lambda c: at[1][:, c, tok],
                                lambda c: wp[0][:, 2, c, :], lambda c: wp[1][:, 2, c, :])
                ins.then_inc(fillA[2 + n], 1)

            def XT(g, n):
                wait_free(pe, g, 0, "XT", 0)
                wait_free(pe, g, 1, "XT", 0)
                for i in range(GT):
                    pe.wait_ge(xn_ready, g * GT + i + 1)
                    for c in range(KC):
                        ins = tr(A[c][:, i * P:(i + 1) * P], xn[:, i % 2, c * P:(c + 1) * P], ident[:, :])
                        if i == GT - 1:
                            ins.then_inc(fillA[c], 1)
                        if c == KC - 1 and i < GT - 1:
                            ins.then_inc(xn_used, 1)

            def Q(g, c):
                if c == 0:
                    wait_drained(pe, g, 0, "XT", 0)
                    wait_drained(pe, g, 1, "XT", 0)
                wait_free(pe, g, 2 + c, "Q", c)
                three(A[2 + c][:, :], *proj(0, c), lambda k: at[0][:, k, :], lambda k: at[1][:, k, :]).then_inc(fillA[2 + c], 1)

            def Sc(g, i):
                if i == 0:
                    wait_drained(pe, g, 0, "K", 0)
                    wait_drained(pe, g, 1, "K", 1)
                    wait_drained(pe, g, 2, "Q", 0)
                    wait_drained(pe, g, 3, "Q", 1)
                for c in range(KC):
                    for b in range(4):
                        if c == 0:
                            wait_free(pe, g, b, "S", i)
                        rows = slice(32 * b, 32 * b + 32)
                        ins = mm(A[b][:, c * 2 * P:(c + 1) * 2 * P], qt[rows, c, i * P:(i + 1) * P],
                                 km[rows, c, i, :, :].rearrange("p e n -> p (e n)"), start=True, stop=True)
                        if c == KC - 1:
                            ins.then_inc(fillA[b], 1)

            def Tr(g, i):
                for b in range(4):
                    wait_free(pe, g, b, "T", i)
                    for k in range(4):
                        ins = tr(A[b][:, k * P:(k + 1) * P], pr[:, 4 * b + k, :], ident[:, :])
                    ins.then_inc(fillA[b], 1)

            def PV(g, i):
                pe.wait_ge(v_parts, g * 2 + i // 2 + 1)
                for b in range(2):
                    wait_free(pe, g, b, "PV", i)
                    for k in range(NH // 2):
                        j = b * (NH // 2) + k
                        if k % 4 == 0:
                            wait_drained(pe, g, j // 4, "T", i)
                        dst = A[b][:, k * VW:(k + 1) * VW]
                        mm(dst, ph[:, j, :], vp[:, i, j, :], start=True, stop=False)
                        ins = mm(dst, pl[:, j, :], vp[:, i, j, :], start=False, stop=True)
                    ins.then_inc(fillA[b], 1)

            def OT(g, i):
                pe.wait_ge(o_ready, g * GT + i + 1)
                wait_free(pe, g, 2, "OT", i)
                of = o[:, :, :].rearrange("p h d -> p (h d)")
                for c in range(KC):
                    ins = tr(A[2][:, c * P:(c + 1) * P], of[:, c * P:(c + 1) * P], ident[:, :])
                ins.then_inc(fillA[2], 1)

            def OP(g, i):
                wait_drained(pe, g, 2, "OT", i)
                wait_free(pe, g, 3, "OP", i)
                three(A[3][:, 0:E], lambda c: ot[0][:, c, :], lambda c: ot[1][:, c, :],
                      lambda c: wp[0][:, 3, c, :], lambda c: wp[1][:, 3, c, :]).then_inc(fillA[3], 1)

            def XT2(g, i):
                pe.wait_ge(xn2_ready, g * GT + i + 1)
                wait_free(pe, g, 2, "XT2", i)
                for c in range(KC):
                    ins = tr(A[2][:, c * P:(c + 1) * P], xn2[:, c * P:(c + 1) * P], ident[:, :])
                ins.then_inc(fillA[2], 1)

            def RT(g, i):
                wait_drained(pe, g, 2, "XT2", i)
                wait_free(pe, g, 3, "RT", i)
                for c in range(KC):
                    ins = mm(A[3][:, 0:NRT], t32[:, c, :], wr[:, c, :], start=c == 0, stop=c == KC - 1)
                ins.then_inc(fillA[3], 1)

            def GTr(g, n):
                pe.wait_ge(gates, g + 1)
                wait_free(pe, g, 2, "GT", 0)
                for i in range(GT):
                    ins = tr(A[2][0:2 * NRT, i * P:(i + 1) * P], gs[:, i, :].bitcast(F32), ident[:, :])
                ins.then_inc(fillA[2], 1)

            def UP(f, p, r):
                if r == 0:
                    pe.wait_ge(x2_lo, (f + 1) * GT)
                    wait(pe, fin_add, f * 2)
                if r >= 1:
                    pe.wait_ge(gelu, f * NX + r)
                three(U[:, :], lambda c: wu[0][:, c, r, :], lambda c: wu[1][:, c, r, :],
                      lambda c: x2[p][0][:, c, :], lambda c: x2[p][1][:, c, :]).then_inc(upF, 1)
                if r >= NSH:
                    if r == NSH:
                        wait_drained(pe, f, 2, "GT", 0)
                    else:
                        pe.wait_ge(gated, f * NRT + r - NSH)
                    e = r - NSH
                    mm(W[:, :], sel[:, e:e + 1].broadcast_to([P, P]), gt[p][:, :], start=True, stop=True).then_inc(bcast, 1)

            def DN(f, p, r):
                pe.wait_ge(h_lo, f * NX + r + 1)
                if r == 0:
                    wait(pe, f_evict, f * 2)
                for c in range(KC):
                    for k, (w, h) in enumerate(((wd[0], hh), (wd[0], hl), (wd[1], hh))):
                        ins = mm(FB[c][:, :], w[:, r, c * P:(c + 1) * P], h[:, r % 3, :],
                                 start=r == 0 and k == 0, stop=r == NX - 1 and k == 2)
                ins.then_inc(dn_done, 1)

            def FIN(f, p, n):
                pe.wait_ge(f_evict, f * 2 + 2)
                pe.wait_ge(gelu, (f + 1) * NX)
                pe.wait_ge(gated, (f + 1) * NRT)
                for b, bank in enumerate((U, W)):
                    for k in range(2):
                        for c in range(KC):
                            i = 2 * b + k
                            ins = tr(bank[:, k * E + c * P:k * E + (c + 1) * P], ft[:, c, i * P:(i + 1) * P], ident[:, :])
                    ins.then_inc(fin_fill, 1)

            attn = {"K": K, "V": V, "XT": XT, "Q": Q, "S": Sc, "T": Tr, "PV": PV, "OT": OT, "OP": OP,
                    "XT2": XT2, "RT": RT, "GT": GTr}
            experts = {"UP": UP, "DN": DN, "FIN": FIN}

            def both(stages, g, p=None):
                p = g % 2 if p is None else p
                for name, n in stages:
                    if name in attn:
                        attn[name](g, n)
                    elif name in experts:
                        experts[name](g - 1, 1 - p, n)

            pe.wait_ge(const, 1)
            pe.wait_ge(dve_const, 1)
            pe.wait_ge(w_split, NP)
            pe.wait_ge(router_in, 16)
            run_steps(pe, both)

        @block.scalar
        def _(act_e):
            ac = nc.scalar.activation

            def XT(g, n):
                for c in range(KC):
                    wait_filled(act_e, g, c, "XT", 0)
                    ac(at[0][:, c, :], A[c][:, :], ACT.Copy).then_inc(xt_hi, 1)

            def Q(g, c):
                wait_filled(act_e, g, 2 + c, "Q", c)
                ac(qt[:, c, :], A[2 + c][:, :], ACT.Copy).then_inc(drainA[2 + c], 1)

            def Sc(g, i):
                for b in range(4):
                    act_e.wait_ge(nm_ready, g * 16 + 4 * i + b + 1)
                    for k in range(4):
                        j = 4 * b + k
                        ins = ac(pr[:, j, :], A[b][:, k * P:(k + 1) * P], ACT.Exp, bias=nm[:, j:j + 1], scale=SCALE)
                    ins.then_inc(drainA[b], 1)

            def Tr(g, i):
                for b in range(4):
                    wait_filled(act_e, g, b, "T", i)
                    ac(ph[:, 4 * b:4 * b + 4, :].rearrange("p h t -> p (h t)"), A[b][:, :], ACT.Copy).then_inc(p_hi, 1)

            def OT(g, i):
                wait_filled(act_e, g, 2, "OT", i)
                ac(ot[0][:, :, :].rearrange("p c t -> p (c t)"), A[2][:, 0:E], ACT.Copy).then_inc(ot_hi, 1)

            def XT2(g, i):
                wait_filled(act_e, g, 2, "XT2", i)
                wait(act_e, x2_lo, g * GT + i)
                ac(t32[:, :, :].rearrange("p c t -> p (c t)"), A[2][:, 0:E], ACT.Copy).then_inc(drainA[2], 1)

            def ROUTE(g, n):
                act_e.wait_ge(rt_step, g * KR + 2)
                for i in range(GT):
                    ins = ac(ex[:, i, :], lg[:, i, :], ACT.Exp, bias=nlm[:, i:i + 1])
                ins.then_inc(rt_exp, 1)

            def GTr(g, p):
                wait_filled(act_e, g, 2, "GT", 0)
                ac(gt[p][0:2 * NRT, :], A[2][0:2 * NRT, :], ACT.Copy).then_inc(drainA[2], 1)

            def UP(f, r):
                act_e.wait_ge(upF, f * NX + r + 1)
                wait(act_e, h_lo, f * NX + r - 2)
                ac(act[:, r % 3, :], U[:, :], ACT.Gelu).then_inc(gelu, 1)

            def FIN(f, n):
                act_e.wait_ge(dn_done, (f + 1) * NX)
                for c in range(KC):
                    ac(ft[:, c, :], FB[c][:, :], ACT.Copy).then_inc(f_evict, 1)

            attn = {"XT": XT, "Q": Q, "S": Sc, "T": Tr, "OT": OT, "XT2": XT2, "ROUTE": ROUTE}
            experts = {"UP": UP, "FIN": FIN}

            def both(stages, g, p=None):
                p = g % 2 if p is None else p
                for name, n in stages:
                    if name == "GT":
                        GTr(g, p)
                    elif name in attn:
                        attn[name](g, n)
                    elif name in experts:
                        experts[name](g - 1, n)

            act_e.wait_ge(w_split, NP)
            act_e.wait_ge(dve_const, 1)
            run_steps(act_e, both)

        @block.vector
        def _(dve):
            v = nc.vector

            v.memset(vp[:, :, :, :].rearrange("p t h v -> p (t h v)"), 0.0).then_inc(const0, 1)
            for p in range(2):
                v.memset(gt[p][:, :].bitcast(F32), 0.0)
            v.memset(neg_half[:, :], -0.5)
            v.memset(mask[:, 0:1], 0.0)
            v.memset(mask[:, 1:2], 1.0).then_inc(const0, 1)
            dve.wait_ge(const0, 2)
            for q in range(4):
                v.memset(mask[32 * q:32 * q + HD, 0:1], 1.0)
                v.memset(mask[32 * q:32 * q + HD, 1:2], 0.0)
            for k in range(TOPK):
                v.memset(prob[:, :, NRT + k:NRT + k + 1], -1.0 - k)
            v.memset(vp[:, :, :, HD:HD + 1], 1.0)
            dve.wait_ge(sel_set, 2)
            v.tensor_copy(sel[:, :], self32[:, :]).then_inc(dve_const, 1)

            count = [0, 0]
            hi = 0
            for n in range(NP):
                count[n % 2] += 16 * len(PIECES[n])
                dve.wait_ge(w_in[n % 2], count[n % 2])
                jobs = [(staged(n, off, shape), [part(t) for t in TARGET[n](m)])
                        for (m, off), _, part, shape in PIECES[n]]
                for src, (h, _) in jobs:
                    v.tensor_copy(h, src).then_inc(w_hi, 1)
                hi += len(jobs)
                dve.wait_ge(w_hi, hi)
                for src, (h, l) in jobs:
                    ins = v.tensor_tensor(l, src, h.bitcast(F32), ALU.subtract)
                ins.then_inc(w_split, 1)

            def CTX(g, n):
                dve.wait_ge(ctx_in, (g + 1) * 16)
                wait(dve, fillA[3], (g - 1) * KA[3] + nth_use(3, "Q", 1))
                v.tensor_copy(at[0][:, :, :], cg[:, :, :]).then_inc(ctx_hi, 1)

            def K(g, c):
                wait_filled(dve, g, c, "K", c)
                src = A[c][:, :].rearrange("p (i t) -> p i t", i=GT)
                v.tensor_scalar(km[:, c, :, 0, :], src, mask[:, 0:1], None, ALU.mult)
                v.tensor_scalar(km[:, c, :, 1, :], src, mask[:, 1:2], None, ALU.mult).then_inc(drainA[c], 1)

            def V(g, n):
                b = 2 + n
                wait_filled(dve, g, b, "V", n)
                wait(dve, v_parts, (g - 1) * 2 + n + 1)
                for k in range(2):
                    ins = v.tensor_copy(vp[:, 2 * n + k, :, 0:HD],
                                        A[b][:, k * E:(k + 1) * E].rearrange("p (h d) -> p h d", h=NH))
                ins.then_inc(v_hi, 1)
                dve.wait_ge(v_hi, g * 2 + n + 1)
                for k in range(2):
                    ins = v.tensor_tensor(vrest[:, n, k * E:(k + 1) * E].rearrange("p (h d) -> p h d", h=NH),
                                          A[b][:, k * E:(k + 1) * E].rearrange("p (h d) -> p h d", h=NH),
                                          vp[:, 2 * n + k, :, 0:HD], ALU.subtract)
                ins.then_inc(drainA[b], 1)
                wait_drained(dve, g, b, "V", n)
                for k in range(2):
                    ins = v.tensor_copy(vp[:, 2 * n + k, :, VP:VP + HD],
                                        vrest[:, n, k * E:(k + 1) * E].rearrange("p (h d) -> p h d", h=NH))
                ins.then_inc(v_mid, 1)

            def LN1(g, p, h):
                dve.wait_ge(x_in[p], (h + 1) * 16)
                for i in range(GT):
                    ins = v.bn_stats(st1[:, i, :], xy[p][:, i, :])
                ins.then_inc(ln1_st, 1)
                wait_apart(ln1_st, g + 1)
                for i in range(GT):
                    ins = v.bn_aggr(mv1[:, i, :], st1[:, i, :])
                ins.then_inc(ln1_mv, 1)
                dve.wait_ge(ln1_mv, g + 1)
                v.tensor_scalar(ve1[:, :], mv1[:, :, 1], EPS, None, ALU.add).then_inc(ln1_ve, 1)

            def XT(g, p):
                dve.wait_ge(ln1_rs, g + 1)
                for i in range(GT):
                    if i < 2:
                        wait(dve, xn_used, g * (GT - 1))
                    else:
                        dve.wait_ge(xn_used, g * (GT - 1) + i - 1)
                    v.tensor_scalar(xn[:, i % 2, :], xy[p][:, i, :], mv1[:, i, 0:1], rs1[:, i:i + 1],
                                    ALU.subtract, ALU.mult).then_inc(xn_ready, 1)
                for c in range(KC):
                    dve.wait_ge(xt_hi, g * KC + c + 1)
                    v.tensor_tensor(at[1][:, c, :], A[c][:, :], at[0][:, c, :].bitcast(F32), ALU.subtract)\
                        .then_inc(drainA[c], 1)

            def Sc(g, i):
                for b in range(4):
                    wait_filled(dve, g, b, "S", i)
                    v.reduce_max(mx[:, 4 * b:4 * b + 4], A[b][:, :].rearrange("p (h t) -> p h t", h=4), AX.X)\
                        .then_inc(mx_ready, 1)
                    dve.wait_ge(mx_ready, g * 16 + 4 * i + b + 1)
                    v.tensor_scalar(nm[:, 4 * b:4 * b + 4], mx[:, 4 * b:4 * b + 4], -SCALE, None, ALU.mult)\
                        .then_inc(nm_ready, 1)

            def Tr(g, i):
                for b in range(4):
                    dve.wait_ge(p_hi, g * 16 + 4 * i + b + 1)
                    hs = slice(4 * b, 4 * b + 4)
                    v.tensor_tensor(pl[:, hs, :].rearrange("p h t -> p (h t)"), A[b][:, :],
                                    ph[:, hs, :].rearrange("p h t -> p (h t)"), ALU.subtract).then_inc(drainA[b], 1)

            def PV(g, i):
                for b in range(2):
                    wait_filled(dve, g, b, "PV", i)
                    hs = slice(b * NH // 2, (b + 1) * NH // 2)
                    v.tensor_reduce(od[:, hs, :],
                                    A[b][:, 0:NH // 2 * VW].rearrange("p (h q e) -> p h e q", h=NH // 2, q=3),
                                    AX.X, ALU.add).then_inc(drainA[b], 1)
                for b in range(2):
                    wait_drained(dve, g, b, "PV", i)
                v.reciprocal(rd[:, :], od[:, :, HD]).then_inc(rd_ready, 1)
                dve.wait_ge(rd_ready, g * GT + i + 1)
                v.tensor_tensor(o[:, :, :], od[:, :, 0:HD], rd[:, :].unsqueeze(2).broadcast_to([P, NH, HD]), ALU.mult)\
                    .then_inc(o_ready, 1)

            def OT(g, i):
                dve.wait_ge(ot_hi, g * GT + i + 1)
                v.tensor_tensor(ot[1][:, :, :].rearrange("p c t -> p (c t)"), A[2][:, 0:E],
                                ot[0][:, :, :].rearrange("p c t -> p (c t)").bitcast(F32), ALU.subtract)\
                    .then_inc(drainA[2], 1)

            def OP(g, p, i):
                wait_filled(dve, g, 3, "OP", i)
                v.tensor_tensor(xy[p][:, i, :], A[3][:, 0:E], xy[p][:, i, :], ALU.add).then_inc(drainA[3], 1)
                wait_drained(dve, g, 3, "OP", i)
                v.bn_stats(st2[:, :], xy[p][:, i, :]).then_inc(ln2_st, 1)
                wait_apart(ln2_st, g * GT + i + 1)
                v.bn_aggr(mv2[:, :], st2[:, :]).then_inc(ln2_mv, 1)
                dve.wait_ge(ln2_mv, g * GT + i + 1)
                v.tensor_scalar(ve2[:, :], mv2[:, 1:2], EPS, None, ALU.add).then_inc(ln2_ve, 1)

            def OP_norm(g, p, i):
                dve.wait_ge(ln2_rs, g * GT + i + 1)
                v.tensor_scalar(xn2[:, :], xy[p][:, i, :], mv2[:, 0:1], rs2[:, 0:1], ALU.subtract, ALU.mult)\
                    .then_inc(xn2_ready, 1)

            def XT2(g, p, i):
                wait_drained(dve, g, 2, "XT2", i)
                dst = slice(i * P, (i + 1) * P)
                v.tensor_copy(x2[p][0][:, :, dst], t32[:, :, :]).then_inc(x2_hi, 1)
                dve.wait_ge(x2_hi, g * GT + i + 1)
                v.tensor_tensor(x2[p][1][:, :, dst], t32[:, :, :], x2[p][0][:, :, dst].bitcast(F32), ALU.subtract)\
                    .then_inc(x2_lo, 1)

            def RT(g, i):
                wait_filled(dve, g, 3, "RT", i)
                v.tensor_copy(lg[:, i, :], A[3][:, 0:NRT]).then_inc(drainA[3], 1)

            def ROUTE(g, n):
                done = [g * KR]

                def link(ins):
                    done[0] = done[0] + 1
                    ins.then_inc(rt_step, 1)
                    wait_apart(rt_step, done[0])

                wait_apart(drainA[3], g * KA[3] + nth_use(3, "RT", GT - 1))
                for i in range(GT):
                    ins = v.max(lm[:, i, :], lg[:, i, :])
                link(ins)
                link(v.tensor_scalar(nlm[:, :], lm[:, :, 0], -1.0, None, ALU.mult))
                dve.wait_ge(rt_exp, g + 1)
                link(v.reduce_sum(rsum[:, :], ex[:, :, :], AX.X))
                link(v.reciprocal(rrec[:, :], rsum[:, :]))
                link(v.tensor_tensor(prob[:, :, 0:NRT], ex[:, :, :],
                                     rrec[:, :].unsqueeze(2).broadcast_to([P, GT, NRT]), ALU.mult))
                for i in range(GT):
                    ins = v.max(top[:, i, :], prob[:, i, 0:NRT])
                link(ins)
                link(v.tensor_copy(top[:, :, TOPK:8], prob[:, :, NRT:NRT + TOPK]))
                for i in range(GT):
                    ins = v.match_replace(rest[:, i, :], top[:, i, :], prob[:, i, :], 0.0)
                link(ins)
                v.tensor_tensor(gate[:, :, :], prob[:, :, 0:NRT], rest[:, :, 0:NRT], ALU.subtract).then_inc(gate_set, 1)
                dve.wait_ge(gate_set, g * 2 + 1)
                v.tensor_copy(gs[:, :, 0:NRT], gate[:, :, :]).then_inc(gate_set, 1)
                dve.wait_ge(gate_set, g * 2 + 2)
                v.tensor_tensor(gs[:, :, NRT:2 * NRT], gate[:, :, :], gs[:, :, 0:NRT].bitcast(F32), ALU.subtract)\
                    .then_inc(gates, 1)

            def UP(f, r):
                s = r % 3
                dve.wait_ge(gelu, f * NX + r + 1)
                if r >= NSH:
                    dve.wait_ge(bcast, f * NRT + r - NSH + 1)
                    v.tensor_tensor(act[:, s, :], W[:, :], act[:, s, :], ALU.mult).then_inc(gated, 1)
                    dve.wait_ge(gated, f * NRT + r - NSH + 1)
                wait(dve, dn_done, f * NX + r - 2)
                v.tensor_copy(hh[:, s, :], act[:, s, :]).then_inc(h_hi, 1)

            def FIN(f, p, n):
                wait(dve, stored, f * 32)
                for b, bank in enumerate((U, W)):
                    dve.wait_ge(fin_fill, f * 2 + b + 1)
                    v.tensor_tensor(ob[:, 2 * b:2 * b + 2, :].rearrange("p i e -> p (i e)"), bank[:, :],
                                    xy[p][:, 2 * b:2 * b + 2, :].rearrange("p i e -> p (i e)"), ALU.add)\
                        .then_inc(fin_add, 1)

            attn = {"CTX": CTX, "K": K, "V": V, "S": Sc, "T": Tr, "PV": PV, "OT": OT, "RT": RT, "ROUTE": ROUTE}

            def both(stages, g, p=None):
                h = g // 2 if p is None else half_of[0]
                p = g % 2 if p is None else p
                for name, n in stages:
                    if name == "LN1":
                        LN1(g, p, h)
                    elif name == "XT":
                        XT(g, p)
                    elif name == "OP":
                        OP(g, p, n)
                        OP_norm(g, p, n)
                    elif name == "XT2":
                        XT2(g, p, n)
                    elif name in attn:
                        attn[name](g, n)
                    elif name == "UP":
                        UP(g - 1, n)
                    elif name == "FIN":
                        FIN(g - 1, 1 - p, n)

            half_of = [None]
            both(ATTN_ONLY, 0)
            both(STEP, 1)
            with dve.Fori(0, (G - 2) // 2) as i:
                half_of[0] = i + 1
                both(STEP, i * 2 + 2, 0)
                both(STEP, i * 2 + 3, 1)
            both(EXPERTS_ONLY, G)

        @block.gpsimd
        def _(pool):
            q = nc.gpsimd
            q.memset(ident[:, :], 0.0)
            q.memset(self32[:, :], 0.0).then_inc(pool_set, 1)
            pool.wait_ge(pool_set, 1)
            q.affine_select(out=ident[:, :], in_=ident[:, :], compare_op=ALU.not_equal, fill=1.0,
                            base=0, pattern=[[-1, P]], channel_multiplier=1).then_inc(const, 1)
            for k in range(2):
                q.affine_select(out=self32[:, :], in_=self32[:, :], compare_op=ALU.not_equal, fill=1.0,
                                base=-k * NRT, pattern=[[-1, NRT]], channel_multiplier=1).then_inc(sel_set, 1)
                pool.wait_ge(sel_set, k + 1)
            pool.wait_ge(dve_const, 1)

            def CTX(g, n):
                pool.wait_ge(ctx_hi, g + 1)
                q.tensor_tensor(at[1][:, :, :], cg[:, :, :], at[0][:, :, :].bitcast(F32), ALU.subtract).then_inc(ctx_lo, 1)

            def V(g, n):
                pool.wait_ge(v_mid, g * 2 + n + 1)
                for k in range(2):
                    ins = q.tensor_tensor(vp[:, 2 * n + k, :, 2 * VP:2 * VP + HD],
                                          vrest[:, n, k * E:(k + 1) * E].rearrange("p (h d) -> p h d", h=NH),
                                          vp[:, 2 * n + k, :, VP:VP + HD], ALU.subtract)
                ins.then_inc(v_parts, 1)

            def LN1(g, n):
                pool.wait_ge(ln1_ve, g + 1)
                q.tensor_tensor(rs1[:, :], ve1[:, :], neg_half[:, :], ALU.pow).then_inc(ln1_rs, 1)

            def OP(g, i):
                pool.wait_ge(ln2_ve, g * GT + i + 1)
                q.tensor_tensor(rs2[:, :], ve2[:, :], neg_half[:, 0:1], ALU.pow).then_inc(ln2_rs, 1)

            def UP(f, r):
                s = r % 3
                pool.wait_ge(h_hi, f * NX + r + 1)
                q.tensor_tensor(hl[:, s, :], act[:, s, :], hh[:, s, :].bitcast(F32), ALU.subtract).then_inc(h_lo, 1)

            attn = {"CTX": CTX, "V": V, "LN1": LN1, "OP": OP}

            def both(stages, g, p=None):
                for name, n in stages:
                    if name in attn:
                        attn[name](g, n)
                    elif name == "UP":
                        UP(g - 1, n)

            run_steps(pool, both)


def transposed_weights(inputs):
    import numpy as np

    def c(a):
        return np.ascontiguousarray(a)

    def heads(w):
        w = np.asarray(w).reshape(4, 2, 2, HD, E).transpose(1, 0, 2, 3, 4)
        return c(w.reshape(E, E).T)

    return {
        "wq": heads(inputs["L0_xattn_Wq"]),
        "wk": heads(inputs["L0_xattn_Wk"]),
        "wv": c(np.asarray(inputs["L0_xattn_Wv"]).T),
        "wo": c(np.asarray(inputs["L0_xattn_Wo"]).T),
        "sup": c(np.asarray(inputs["L0_ffn_shared_up"]).transpose(2, 0, 1)),
        "sdn": c(np.asarray(inputs["L0_ffn_shared_down"]).transpose(2, 0, 1)),
        "rup": c(np.asarray(inputs["L0_ffn_routed_up"]).transpose(2, 0, 1)),
        "rdn": c(np.asarray(inputs["L0_ffn_routed_down"]).transpose(2, 0, 1)),
        "rw": c(np.asarray(inputs["L0_ffn_router_w"]).T),
    }


def kernel(**inputs):
    import numpy as np
    import concourse.bacc as bacc
    from concourse.bass_utils import run_bass_kernel_spmd

    nc = bacc.Bacc("TRN2", target_bir_lowering=False, num_devices=1)
    arrays = {"x": np.ascontiguousarray(inputs["x"]),
              "ctx_t": np.ascontiguousarray(np.asarray(inputs["ctx_1024"]).reshape(B * S, E).T)}
    arrays.update(transposed_weights(inputs))
    args = [nc.dram_tensor(f"in_{k}", a.shape, mybir.dt.from_np(a.dtype), kind="ExternalInput").ap()
            for k, a in arrays.items()]
    out = nc.dram_tensor("out", (B, S, E), F32, kind="ExternalOutput").ap()
    program(nc, *args, out)
    r = run_bass_kernel_spmd(nc, [{f"in_{k}": a for k, a in arrays.items()}], core_ids=[0])
    return r.results[0]["out"]
```
